# Optimizing a Trainium2 kernel written in Bass

```python
import numpy as np
import jax
import jax.numpy as jnp

def _softmax(x, axis=-1):
    return jax.nn.softmax(x, axis=axis)

def _gelu(x):
    return jax.nn.gelu(x, approximate=True)

def _silu(x):
    return jax.nn.silu(x)

def _sigmoid(x):
    return jax.nn.sigmoid(x)

def _layernorm(x, axis=-1, eps=1e-05):
    m = jnp.mean(x, axis=axis, keepdims=True)
    v = jnp.var(x, axis=axis, keepdims=True)
    return (x - m) / jnp.sqrt(v + eps)

def _scatter_add(tgt, idx, src, axis=0):
    return tgt.at[idx].add(src)

def _segment_sum(src, seg, n):
    return jax.ops.segment_sum(src, seg, n)
kernel_name = 'mk_adj_preln_d2_adj_r2_5cc257'

def setup_inputs(seed: int=0):
    np.random.seed(seed)
    _w = jnp.asarray

    def _rec_inputs():
        import jax
        import jax.numpy as jnp
        _gk = jax.random.key(seed)
        x = -0.0001538 + 1 * jax.random.normal(jax.random.fold_in(_gk, 1), (128, 128, 384), jnp.float32)
        _a = jax.random.bernoulli(jax.random.fold_in(_gk, 2), 0.125, (128, 128, 128))
        _a = jnp.logical_or(_a, jnp.swapaxes(_a, -1, -2))
        _a = jnp.logical_or(_a, jnp.eye(128, dtype=bool))
        _af = _a.astype(jnp.float32)
        _af = _af * jax.random.uniform(jax.random.fold_in(_gk, 3), (128, 128, 128), jnp.float32, 0.05, 0.999992)
        adj = _af
        return (x, adj)
    x, adj = _rec_inputs()

    def _L0_gnn_setup():
        import jax, jax.numpy as jnp
        import numpy as np
        B, N, D, H = (8, 512, 384, 12)
        HD = D // H

        def _split_heads(x):
            b, n, _ = x.shape
            return x.reshape(b, n, H, HD).transpose(0, 2, 1, 3)
        key = jax.random.key(seed)
        ks = jax.random.split(key, 10)
        input_graph = jax.random.normal(ks[0], (B, N, D), dtype=jnp.float32)
        u = jax.random.uniform(ks[1], (B, N, N), dtype=jnp.float32)
        keep = jax.random.uniform(ks[2], (B, N, N)) < 0.15
        adj = jnp.where(keep, u, 0.0)
        s = 1.0 / np.sqrt(D)
        Wq = jax.random.normal(ks[3], (D, D), dtype=jnp.float32) * s
        bq = jnp.zeros((D,), dtype=jnp.float32)
        Wk = jax.random.normal(ks[4], (D, D), dtype=jnp.float32) * s
        bk = jnp.zeros((D,), dtype=jnp.float32)
        Wv = jax.random.normal(ks[5], (D, D), dtype=jnp.float32) * s
        bv = jnp.zeros((D,), dtype=jnp.float32)
        beta = jnp.asarray(0.1, dtype=jnp.float32)
        return {'input_graph': input_graph, 'adj': adj, 'Wq': Wq, 'bq': bq, 'Wk': Wk, 'bk': bk, 'Wv': Wv, 'bv': bv, 'beta': beta}
    _L0_gnn_all = _L0_gnn_setup()
    _L0_gnn_in = {k: v for k, v in _L0_gnn_all.items() if k in ('Wq', 'bq', 'Wk', 'bk', 'Wv', 'bv', 'beta')}
    del _L0_gnn_all

    def _L1_gnn_setup():
        import jax, jax.numpy as jnp
        import numpy as np
        NUM_HEADS = 12
        HIDDEN = 384
        HEAD = HIDDEN // NUM_HEADS
        SCALE = HIDDEN ** (-0.5)
        key = jax.random.key(seed)
        ks = jax.random.split(key, 8)
        B, N = (16, 256)
        std = HIDDEN ** (-0.5)
        return {'x': jax.random.normal(ks[0], (B, N, HIDDEN), dtype=jnp.float32), 'encoding_bias': jax.random.normal(ks[1], (B, N, N), dtype=jnp.float32), 'Wq': jax.random.normal(ks[2], (HIDDEN, HIDDEN), dtype=jnp.float32) * std, 'Wk': jax.random.normal(ks[3], (HIDDEN, HIDDEN), dtype=jnp.float32) * std, 'Wv': jax.random.normal(ks[4], (HIDDEN, HIDDEN), dtype=jnp.float32) * std, 'bv': jax.random.normal(ks[5], (HIDDEN,), dtype=jnp.float32) * 0.01, 'Wo': jax.random.normal(ks[6], (HIDDEN, HIDDEN), dtype=jnp.float32) * std, 'bo': jax.random.normal(ks[7], (HIDDEN,), dtype=jnp.float32) * 0.01}
    _L1_gnn_all = _L1_gnn_setup()
    _L1_gnn_in = {k: v for k, v in _L1_gnn_all.items() if k in ('Wq', 'Wk', 'Wv', 'bv', 'Wo', 'bo')}
    del _L1_gnn_all
    return {'x': x, 'adj': adj, 'L0_gnn_Wq': _L0_gnn_in['Wq'], 'L0_gnn_bq': _L0_gnn_in['bq'], 'L0_gnn_Wk': _L0_gnn_in['Wk'], 'L0_gnn_bk': _L0_gnn_in['bk'], 'L0_gnn_Wv': _L0_gnn_in['Wv'], 'L0_gnn_bv': _L0_gnn_in['bv'], 'L0_gnn_beta': _L0_gnn_in['beta'], 'L1_gnn_Wq': _L1_gnn_in['Wq'], 'L1_gnn_Wk': _L1_gnn_in['Wk'], 'L1_gnn_Wv': _L1_gnn_in['Wv'], 'L1_gnn_bv': _L1_gnn_in['bv'], 'L1_gnn_Wo': _L1_gnn_in['Wo'], 'L1_gnn_bo': _L1_gnn_in['bo']}

def reference(x, adj, L0_gnn_Wq, L0_gnn_bq, L0_gnn_Wk, L0_gnn_bk, L0_gnn_Wv, L0_gnn_bv, L0_gnn_beta, L1_gnn_Wq, L1_gnn_Wk, L1_gnn_Wv, L1_gnn_bv, L1_gnn_Wo, L1_gnn_bo):
    import jax
    import jax.numpy as jnp

    def _L0_gnn_ref(input_graph, adj, Wq, bq, Wk, bk, Wv, bv, beta):
        import jax, jax.numpy as jnp
        import numpy as np
        B, N, D, H = (8, 512, 384, 12)
        HD = D // H

        def _split_heads(x):
            b, n, _ = x.shape
            return x.reshape(b, n, H, HD).transpose(0, 2, 1, 3)
        q = _split_heads(input_graph @ Wq + bq)
        k = _split_heads(input_graph @ Wk + bk)
        v = _split_heads(input_graph @ Wv + bv)
        scores = jnp.einsum('bhqd,bhkd->bhqk', q, k) / jnp.sqrt(jnp.asarray(HD, input_graph.dtype))
        adj_e = adj[:, None, :, :]
        scores = scores + beta * adj_e
        scores = jnp.where(adj_e > 0, scores, jnp.asarray(-9000000000000000.0, scores.dtype))
        probs = jax.nn.softmax(scores, axis=-1)
        out = jnp.einsum('bhqk,bhkd->bhqd', probs, v)
        return out.transpose(0, 2, 1, 3).reshape(input_graph.shape[0], input_graph.shape[1], D)

    def _L1_gnn_ref(x, encoding_bias, Wq, Wk, Wv, bv, Wo, bo):
        import jax, jax.numpy as jnp
        import numpy as np
        NUM_HEADS = 12
        HIDDEN = 384
        HEAD = HIDDEN // NUM_HEADS
        SCALE = HIDDEN ** (-0.5)
        B, N, _ = x.shape
        q = (x @ Wq.T).reshape(B, N, NUM_HEADS, HEAD)
        k = (x @ Wk.T).reshape(B, N, NUM_HEADS, HEAD)
        v = (x @ Wv.T + bv).reshape(B, N, NUM_HEADS, HEAD)
        a = jnp.einsum('bnhd,bmhd->bhnm', q, k) * SCALE + encoding_bias[:, None, :, :]
        pad_mask = jnp.all(a == 0, axis=-1)
        a = jnp.where(pad_mask[..., None], -jnp.inf, a)
        a = jax.nn.softmax(a, axis=-1)
        a = jnp.nan_to_num(a)
        o = jnp.einsum('bhnm,bmhd->bnhd', a, v).reshape(B, N, HIDDEN)
        return o @ Wo.T + bo
    h = jnp.maximum(_layernorm(x, axis=-1), 0.0)
    x = x + _L0_gnn_ref(h, adj, L0_gnn_Wq, L0_gnn_bq, L0_gnn_Wk, L0_gnn_bk, L0_gnn_Wv, L0_gnn_bv, L0_gnn_beta)
    h = jnp.maximum(_layernorm(x, axis=-1), 0.0)
    x = x + _L1_gnn_ref(h, adj, L1_gnn_Wq, L1_gnn_Wk, L1_gnn_Wv, L1_gnn_bv, L1_gnn_Wo, L1_gnn_bo)
    return x

_drawn_inputs = setup_inputs


def setup_inputs(seed=0):
    import zlib

    import numpy as np

    out = dict(_drawn_inputs(seed))
    spreads = {'L0_gnn_bq': (0.0, 0.8), 'L0_gnn_bk': (0.0, 0.8), 'L0_gnn_bv': (0.0, 0.1)}
    factors = {'L1_gnn_Wq': 8.0, 'L1_gnn_Wk': 8.0, 'L1_gnn_bv': 5.942, 'L1_gnn_bo': 6.558}
    for name, (base, spread) in spreads.items():
        noise = np.random.default_rng([zlib.crc32(name.encode()), seed]).standard_normal(out[name].shape)
        drawn = base * np.exp(spread * noise) if base else spread * noise
        out[name] = jnp.asarray(drawn.astype(out[name].dtype))
    for name, factor in factors.items():
        out[name] = (out[name] * factor).astype(out[name].dtype)
    return out
```

```python
from contextlib import ExitStack
from itertools import count

import concourse.bass as bass
from concourse import mybir

F32 = mybir.dt.float32
F16 = mybir.dt.float16
ALU = mybir.AluOpType
ACT = mybir.ActivationFunctionType
AX = mybir.AxisListType

GRAPHS, NODES, DIM, HEADS = 128, 128, 384, 12
HEAD = DIM // HEADS
P = 128
KC = DIM // P
HC = P // HEAD
GROUP = 4
GROUPS = GRAPHS // GROUP
UNITS = 2 * GROUPS
TOK = GROUP * NODES
SLOTS = GROUP * KC
JOBS = 2 * KC + GROUP
STACK_DMAS = HC * 3
W_SCALE = 256.0
CARRIERS = 16
EPS = 1e-5
MASKED = -9000000000000000.0
HUGE = 3.0e38
SCALE = (float(HEAD) ** -0.5, float(DIM) ** -0.5)


class Unit:

    def __init__(self, n, layer, group, half, parity):
        self.n, self.layer, self.group, self.half, self.parity = n, layer, group, half, parity


def unit(n):
    if n == UNITS - 1:
        return Unit(n, 1, GROUPS - 1, n // 2, n % 2)
    if n % 2 or n == 0:
        return Unit(n, 0, (n + 1) // 2, n // 2, n % 2)
    return Unit(n, 1, n // 2 - 1, n // 2, 0)


def loop_unit(i, off):
    if off % 2:
        return Unit(i * 2 + off, 0, i + (off + 1) // 2, i + (off - 1) // 2, 1)
    return Unit(i * 2 + off, 1, i + (off // 2 - 1), i + off // 2, 0)


class Phase:

    def __init__(self, attend=None, project=None, norm=None, tail=None, look=None, bias=None, keep=None):
        self.attend, self.project, self.norm, self.tail = attend, project, norm, tail
        self.look, self.bias, self.keep = look, bias, keep


FIRST_LOOP, LAST_LOOP = 2, GROUPS - 3


def before():
    u = unit
    return [
        Phase(norm=u(0)),
        Phase(project=u(0), norm=u(1), look=u(0), bias=0),
        Phase(attend=u(0), project=u(1), look=u(1), bias=1),
        Phase(tail=u(0), norm=u(2)),
        Phase(attend=u(1), project=u(2), norm=u(3), look=u(2), keep=0),
        Phase(attend=u(2), project=u(3), norm=u(4), look=u(3), tail=u(1), bias=2),
    ]


def inside(i):
    return [
        Phase(tail=loop_unit(i, -2), attend=loop_unit(i, -1), project=loop_unit(i, 0),
              look=loop_unit(i, 0), norm=loop_unit(i, 1), keep=i - 1),
        Phase(tail=loop_unit(i, -1), attend=loop_unit(i, 0), project=loop_unit(i, 1),
              look=loop_unit(i, 1), norm=loop_unit(i, 2), bias=i + 1),
    ]


def after():
    u, n = unit, UNITS
    return [
        Phase(tail=u(n - 6), attend=u(n - 5), project=u(n - 4), look=u(n - 4), norm=u(n - 3), keep=GROUPS - 3),
        Phase(tail=u(n - 5), attend=u(n - 4), project=u(n - 3), look=u(n - 3), norm=u(n - 2), bias=GROUPS - 1),
        Phase(tail=u(n - 4), attend=u(n - 3), project=u(n - 2), look=u(n - 2), keep=GROUPS - 2),
        Phase(tail=u(n - 3), norm=u(n - 1)),
        Phase(attend=u(n - 2), project=u(n - 1), look=u(n - 1)),
        Phase(tail=u(n - 2), attend=u(n - 1), keep=GROUPS - 1),
        Phase(tail=u(n - 1)),
    ]


def run_phases(eng, phase):
    for p in before():
        phase(p)
    with eng.Fori(FIRST_LOOP, LAST_LOOP + 1) as i:
        for p in inside(i):
            phase(p)
    for p in after():
        phase(p)


def some(value):
    return not isinstance(value, int) or value > 0


def unit_of_chunk(p, s):
    if s < 0:
        return p.tail, s + SLOTS
    if s >= SLOTS:
        return p.look, s - SLOTS
    return p.attend, s


def finished(p, s, lag):
    u, c = unit_of_chunk(p, s - lag)
    if u is None or c % KC != KC - 1:
        return None, 0
    return u, c // KC


def chunk(u, c):
    return u.n * SLOTS + (c + 1)


def build(nc, x, adj, w0q, b0q, w0k, b0k, w0v, b0v, beta, w1q, w1k, w1v, b1v, w1o, b1o, out):
    weights = (w0q, w0k, w0v, w1q, w1k, w1v, w1o)
    with ExitStack() as ctx:
        def sb(name, shape, dt=F32):
            return ctx.enter_context(nc.sbuf_tensor(name, shape, dt))

        def sem(name):
            return ctx.enter_context(nc.semaphore(name))

        w_hi = [sb(f"w_hi{m}", [P, KC, DIM], F16) for m in range(7)]
        w_lo = [sb(f"w_lo{m}", [P, KC, DIM], F16) for m in range(7)]
        ident = sb("ident", [P, P])
        minus_half = sb("minus_half", [P, 1])
        carrier_p = sb("carrier_p", [P, CARRIERS])
        carrier_v = sb("carrier_v", [P, CARRIERS])
        carried_p, carried_v = count(), count()
        beta_all = sb("beta_all", [P, 1])
        bq_raw = sb("bq_raw", [P, KC])
        bq_cols = sb("bq_cols", [P, KC])
        bk_cols = sb("bk_cols", [P, KC])
        bv_rows = [sb(f"bv_rows{m}", [P, DIM]) for m in range(2)]
        bo_rows = sb("bo_rows", [P, DIM])

        x_norm = sb("x_norm", [P, GROUP, DIM])
        x_res = sb("x_res", [P, GROUP, DIM])
        x_mid = sb("x_mid", [P, GROUP, DIM])
        x_mid_bo = sb("x_mid_bo", [P, GROUP, DIM])
        adj0 = sb("adj0", [P, GROUP, NODES])
        adj1 = sb("adj1", [P, GROUP, NODES])
        mask0 = sb("mask0", [P, GROUP, NODES])
        scaled0 = sb("scaled0", [P, GROUP, NODES])
        bias0 = sb("bias0", [P, GROUP, NODES])

        stats = sb("stats", [P, 6])
        moments = sb("moments", [P, 2])
        shift_var = sb("shift_var", [P, 2, 2])
        rstd = sb("rstd", [P, 1])
        normed = [sb(f"normed{b}", [P, DIM]) for b in range(2)]
        h_hi = [sb(f"h_hi{b}", [P, KC, TOK], F16) for b in range(2)]
        h_lo = [sb(f"h_lo{b}", [P, KC, TOK], F16) for b in range(2)]

        qk32 = [sb(f"qk32{b}", [P, TOK]) for b in range(2)]
        part_hi = [sb(f"part_hi{t}", [P, KC, TOK], F16) for t in range(2)]
        part_lo = [sb(f"part_lo{t}", [P, KC, TOK], F16) for t in range(2)]
        stacked = [[sb(f"stack{t}{b}", [P, HC, KC, TOK], F16) for b in range(2)] for t in range(2)]
        v32 = [sb(f"v32{b}", [P, GROUP, DIM]) for b in range(2)]

        neg = [sb(f"neg{b}", [P, HC, NODES]) for b in range(2)]
        neg_max = sb("neg_max", [P, 2, HEADS])
        neg_min = sb("neg_min", [P, 2, HEADS])
        probs = [sb(f"probs{b}", [P, HC, NODES]) for b in range(2)]
        total = sb("total", [P, 2, HEADS])
        probs_t = [sb(f"probs_t{b}", [P, HC, NODES]) for b in range(2)]
        inv0 = sb("inv0", [P, 2, HEADS])
        inv1 = sb("inv1", [P, HEADS])
        alive = sb("alive", [P, HEADS])
        live = sb("live", [P, HEADS])
        inv_live = sb("inv_live", [P, HEADS])
        inv_wide = sb("inv_wide", [P, HEADS, HEAD])
        o_t = sb("o_t", [P, KC, P])
        o_norm = sb("o_norm", [P, KC, P])
        o_hi = sb("o_hi", [P, KC, P], F16)
        o_lo = sb("o_lo", [P, KC, P], F16)
        o_rows = sb("o_rows", [P, HEADS, HEAD])
        result = [sb(f"result{b}", [P, DIM]) for b in range(GROUP)]

        def bank(name):
            return ctx.enter_context(nc.psum_tensor(name, [P, 512], F32))

        job_bank = [bank("job_bank0"), bank("job_bank1")]
        score_bank = [bank("score_bank0"), bank("score_bank1")]
        pt_bank = [bank("pt_bank0"), bank("pt_bank1")]
        o_bank = bank("o_bank")
        misc_bank = bank("misc_bank")

        consts_in = sem("consts_in")
        weight_in = [sem(f"weight_in{m}") for m in range(7)]
        ident_zero = sem("ident_zero")
        ident_ready = sem("ident_ready")
        half_ready = sem("half_ready")
        bq_ready = sem("bq_ready")
        weight_turned = sem("weight_turned")
        w_hi_ready = sem("w_hi_ready")
        w_lo_ready = sem("w_lo_ready")
        x_norm_in = sem("x_norm_in")
        x_res_in = sem("x_res_in")
        adj0_in = sem("adj0_in")
        adj1_in = sem("adj1_in")
        bias_parts = sem("bias_parts")
        bias_ready = sem("bias_ready")
        stats_done = sem("stats_done")
        moments_done = sem("moments_done")
        shift_ready = sem("shift_ready")
        rstd_done = sem("rstd_done")
        normed_ready = sem("normed_ready")
        h_turned = sem("h_turned")
        h_hi_ready = sem("h_hi_ready")
        h_lo_ready = sem("h_lo_ready")
        job_done = sem("job_done")
        qk32_ready = sem("qk32_ready")
        part_hi_ready = sem("part_hi_ready")
        part_lo_ready = sem("part_lo_ready")
        stack_in = [[sem(f"stack_in{t}{b}") for b in range(2)] for t in range(2)]
        v_ready = sem("v_ready")
        scores_done = sem("scores_done")
        neg_ready = sem("neg_ready")
        min_done = sem("min_done")
        exp_done = sem("exp_done")
        probs_turned = sem("probs_turned")
        probs_t_ready = sem("probs_t_ready")
        pv_done = sem("pv_done")
        inv0_ready = sem("inv0_ready")
        alive_done = sem("alive_done")
        live_done = sem("live_done")
        inv1_done = sem("inv1_done")
        inv_live_done = sem("inv_live_done")
        inv_wide_ready = sem("inv_wide_ready")
        inv_turned = sem("inv_turned")
        o_norm_ready = sem("o_norm_ready")
        o_taken = sem("o_taken")
        o_hi_ready = sem("o_hi_ready")
        o_lo_ready = sem("o_lo_ready")
        post_done = sem("post_done")
        post_taken = sem("post_taken")
        x_mid_ready = sem("x_mid_ready")
        x_mid_bo_ready = sem("x_mid_bo_ready")
        stored = [sem(f"stored{b}") for b in range(GROUP)]

        def staging(m):
            whole = stacked[m % 2][m // 2 % 2][:, :, :, :].rearrange("p h c t -> p (h c t)").bitcast(F32)
            at = (m // 4) * KC * DIM
            return whole[:, at:at + KC * DIM].rearrange("p (c n) -> p c n", c=KC)

        WT_BANKS = score_bank + pt_bank
        x_groups = x.rearrange("(g b) n d -> g n b d", b=GROUP)
        adj_groups = adj.rearrange("(g b) q k -> g q b k", b=GROUP)

        block = ctx.enter_context(nc.Block())

        @block.sync
        def _(sp):
            sp.dma_start(bq_raw[:, :], b0q.rearrange("(c p) -> p c", p=P),
                         allow_slow_non_contiguous=True).then_inc(consts_in, 16)
            sp.dma_start(bk_cols[:, :], b0k.rearrange("(c p) -> p c", p=P),
                         allow_slow_non_contiguous=True).then_inc(consts_in, 16)
            sp.dma_start(beta_all[:, :], beta[0].partition_broadcast(P)).then_inc(consts_in, 16)
            sp.dma_start(x_norm[:, :, :], x_groups[0]).then_inc(x_norm_in, 16)
            for m, w in enumerate(weights):
                sp.dma_start(staging(m), w.rearrange("(c p) n -> p c n", p=P)).then_inc(weight_in[m], 16)
            sp.dma_start(bv_rows[0][:, :], b0v.partition_broadcast(P)).then_inc(consts_in, 16)
            sp.dma_start(bv_rows[1][:, :], b1v.partition_broadcast(P)).then_inc(consts_in, 16)
            sp.dma_start(bo_rows[:, :], b1o.partition_broadcast(P)).then_inc(consts_in, 16)
            sp.dma_start(adj0[:, :, :], adj_groups[0]).then_inc(adj0_in, 16)
            sp.dma_start(x_res[:, :, :], x_groups[0]).then_inc(x_res_in, 16)

            def stack(u, t):
                sp.wait_ge(part_hi_ready, u.n * 2 * KC + (t + 1) * KC)
                if some(u.n * SLOTS - SLOTS):
                    sp.wait_ge(scores_done, u.n * SLOTS - SLOTS)
                sources = ((part_hi, part_lo, part_hi), (part_hi, part_hi, part_lo))[t]
                for low in (False, True):
                    if low:
                        sp.wait_ge(part_lo_ready, u.n * 2 * KC + (t + 1) * KC)
                    for r, part in enumerate(sources):
                        if (part is part_lo) != low:
                            continue
                        for h in range(HC):
                            sp.dma_start(stacked[t][u.parity][HEAD * r:HEAD * (r + 1), h, :, :],
                                         part[t][HEAD * h:HEAD * (h + 1), :, :]).then_inc(
                                             stack_in[t][u.parity], 16)

            def phase(p):
                for s in range(SLOTS):
                    if s == 0 and p.attend is not None and p.attend.layer == 0:
                        g = p.attend.group
                        if not isinstance(g, int) or g + 1 < GROUPS:
                            sp.wait_ge(bias_ready, g + 1)
                            sp.dma_start(adj0[:, :, :], adj_groups[g + 1]).then_inc(adj0_in, 16)
                    if s == 1 and p.look is not None and p.look.layer == 1:
                        u = p.look
                        last = isinstance(u.n, int) and u.n == UNITS - 1
                        if not last:
                            sp.wait_ge(neg_ready, u.n * SLOTS - SLOTS)
                            sp.dma_start(adj1[:, :, :], adj_groups[u.group]).then_inc(adj1_in, 16)
                    if s == 11 and p.look is not None and isinstance(p.look.n, int) and p.look.n == UNITS - 1:
                        sp.wait_ge(neg_ready, p.look.n * SLOTS)
                        sp.dma_start(adj1[:, :, :], adj_groups[p.look.group]).then_inc(adj1_in, 16)
                    if s == 4 and p.project is not None:
                        stack(p.project, 0)
                    if s == 7 and p.project is not None:
                        stack(p.project, 1)
                    if s == 3 and p.tail is not None and p.tail.layer == 0:
                        g = p.tail.group
                        if not isinstance(g, int) or g + 1 < GROUPS:
                            sp.wait_ge(x_mid_ready, g * GROUP + GROUP)
                            sp.dma_start(x_res[:, :, :], x_groups[g + 1]).then_inc(x_res_in, 16)
                    u, b = finished(p, s, 4)
                    if u is not None and u.layer == 1:
                        sp.wait_ge(post_taken, u.n * GROUP + (b + 1))
                        sp.dma_start(out[u.group * GROUP + b, :, :], result[b][:, :]).then_inc(stored[b], 16)
                    if s == 11 and p.norm is not None and p.norm.layer == 0:
                        g = p.norm.group
                        if not isinstance(g, int) or g + 1 < GROUPS:
                            sp.wait_ge(normed_ready, p.norm.n * GROUP + GROUP)
                            sp.dma_start(x_norm[:, :, :], x_groups[g + 1]).then_inc(x_norm_in, 16)

            run_phases(sp, phase)
            for b in range(GROUP):
                sp.wait_ge(stored[b], 16 * GROUPS)

        @block.gpsimd
        def _(pool):
            def carry():
                at = next(carried_p) % CARRIERS
                pool.tensor_tensor(carrier_p[:, at:at + 1], minus_half[:, :], minus_half[:, :], ALU.add)

            pool.memset(ident[:, :], 0.0).then_inc(ident_zero, 1)
            pool.memset(minus_half[:, :], -0.5).then_inc(half_ready, 1)
            pool.wait_ge(ident_zero, 1)
            pool.affine_select(out=ident[:, :], in_=ident[:, :], compare_op=ALU.not_equal, fill=1.0, base=0,
                               pattern=[[-1, P]], channel_multiplier=1).then_inc(ident_ready, 1)
            pool.wait_ge(half_ready, 1)
            pool.wait_ge(consts_in, 96)

            def norm(u, b):
                n = u.n * GROUP + b
                source = x_norm if u.layer == 0 else x_mid
                pool.wait_ge(shift_ready, n + 1)
                pool.tensor_tensor(rstd[:, :], shift_var[:, b % 2, 1:2], minus_half[:, :],
                                   ALU.pow).then_inc(rstd_done, 1)
                if some(n - 1):
                    pool.wait_ge(h_turned, n - 1)
                pool.wait_ge(rstd_done, n + 1)
                carry()
                pool.tensor_scalar(normed[b % 2][:, :], source[:, b, :], shift_var[:, b % 2, 0:1], rstd[:, 0:1],
                                   ALU.add, ALU.mult).then_inc(normed_ready, 1)

            def low_part(u, j):
                n = u.n * 2 * KC + j
                pool.wait_ge(part_hi_ready, n + 1)
                pool.tensor_tensor(part_lo[j // KC][:, j % KC, :], qk32[j % 2][:, :],
                                   part_hi[j // KC][:, j % KC, :], ALU.subtract).then_inc(part_lo_ready, 1)

            def phase(p):
                for s in range(SLOTS):
                    if s % KC == 0 and p.norm is not None:
                        norm(p.norm, s // KC)
                    u, b = finished(p, s, 3)
                    if u is not None and u.layer == 1:
                        pool.wait_ge(o_hi_ready, u.group * GROUP + (b + 1))
                        pool.tensor_tensor(o_lo[:, :, :], o_norm[:, :, :], o_hi[:, :, :],
                                           ALU.subtract).then_inc(o_lo_ready, 1)
                    if p.project is not None and 2 <= s < 2 + 2 * KC:
                        low_part(p.project, s - 2)
                    if p.keep is not None and s in (3, 5, 7, 9):
                        b = (s - 3) // 2
                        pool.wait_ge(post_taken, p.keep * 2 * GROUP + (b + 1))
                        pool.wait_ge(x_mid_ready, p.keep * GROUP + (b + 1))
                        pool.tensor_tensor(x_mid_bo[:, b, :], x_mid[:, b, :], bo_rows[:, :],
                                           ALU.add).then_inc(x_mid_bo_ready, 1)
                    u, b = finished(p, s, KC)
                    if u is not None and u.layer == 0:
                        pool.wait_ge(x_res_in, u.group * 16 + 16)
                        pool.wait_ge(post_taken, u.n * GROUP + (b + 1))
                        if some(u.group * GROUP + (b + 1 - GROUP)):
                            pool.wait_ge(x_mid_bo_ready, u.group * GROUP + (b + 1 - GROUP))
                        pool.tensor_tensor(x_mid[:, b, :], x_res[:, b, :],
                                           o_rows[:, :, :].rearrange("p h d -> p (h d)"),
                                           ALU.add).then_inc(x_mid_ready, 1)

            run_phases(pool, phase)

        @block.scalar
        def _(act):
            for m in range(3):
                act.wait_ge(weight_in[m], 16)
                act.activation(w_hi[m][:, :, :], staging(m), ACT.Copy, scale=W_SCALE).then_inc(w_hi_ready, 1)
            for m in range(3, 7):
                for c in range(KC):
                    n = (m - 3) * KC + c
                    act.wait_ge(weight_turned, n + 1)
                    act.activation(w_hi[m][:, c, :], WT_BANKS[n % 4][:, 0:DIM], ACT.Copy,
                                   scale=W_SCALE).then_inc(w_hi_ready, 1)
            act.wait_ge(bq_ready, 1)
            act.wait_ge(consts_in, 96)

            def exponentials(u, c):
                n = chunk(u, c)
                act.wait_ge(neg_ready, n)
                if some(n - 2):
                    act.wait_ge(probs_turned, n - 2)
                b, first = c // KC % 2, c % KC * HC
                for h in range(HC):
                    last = act.activation(probs[c % 2][:, h, :], neg[c % 2][:, h, :], ACT.Exp,
                                          bias=neg_max[:, b, first + h:first + h + 1], scale=-1.0,
                                          accum_out=total[:, b, first + h:first + h + 1])
                last.then_inc(exp_done, 1)

            def phase(p):
                for s in range(SLOTS):
                    u, c = unit_of_chunk(p, s - 1)
                    if u is not None:
                        n = chunk(u, c)
                        act.wait_ge(probs_turned, n)
                        if some(n - 2):
                            act.wait_ge(pv_done, n - 2)
                        act.activation(probs_t[c % 2][:, :, :].rearrange("p h q -> p (h q)"), pt_bank[c % 2][:, :],
                                       ACT.Copy).then_inc(probs_t_ready, 1)
                    if p.attend is not None:
                        exponentials(p.attend, s)
                    u, b = finished(p, s, 1)
                    if u is not None:
                        act.wait_ge(pv_done, chunk(u, b * KC + KC - 1))
                        if u.layer == 1 and some(u.group * GROUP + b):
                            act.wait_ge(o_norm_ready, u.group * GROUP + b)
                        if u.layer == 0 and b == 0 and some((u.group - 1) * GROUP):
                            act.wait_ge(o_norm_ready, (u.group - 1) * GROUP)
                        if (b == 0) == (u.layer == 1) and some(u.n * GROUP + b):
                            act.wait_ge(post_done, u.n * GROUP + b)
                        act.activation(o_t[:, :, :].rearrange("p c q -> p (c q)"), o_bank[:, 0:DIM],
                                       ACT.Copy).then_inc(o_taken, 1)
                    if s % KC == 2 and p.norm is not None:
                        u, b = p.norm, s // KC
                        act.wait_ge(h_turned, u.n * GROUP + (b + 1))
                        if some(u.n * JOBS - JOBS):
                            act.wait_ge(job_done, u.n * JOBS - JOBS)
                        act.activation(h_hi[u.parity][:, :, P * b:P * (b + 1)],
                                       misc_bank[:, 0:DIM].rearrange("p (c n) -> p c n", c=KC),
                                       ACT.Relu).then_inc(h_hi_ready, 1)
                    if p.project is not None and 1 <= s < 1 + 2 * KC:
                        u, j = p.project, s - 1
                        n = u.n * 2 * KC + j
                        act.wait_ge(job_done, u.n * JOBS + (j + 1))
                        if some(n - 1):
                            act.wait_ge(part_hi_ready, n - 1)
                        if some(n - 1):
                            act.wait_ge(part_lo_ready, n - 1)
                        scale = (SCALE[u.layer] if j < KC else 1.0) / W_SCALE
                        if u.layer == 0:
                            cols = bq_cols if j < KC else bk_cols
                            last = act.activation(qk32[j % 2][:, :], job_bank[j % 2][:, :], ACT.Identity,
                                                  scale=scale, bias=cols[:, j % KC:j % KC + 1])
                        else:
                            last = act.activation(qk32[j % 2][:, :], job_bank[j % 2][:, :], ACT.Copy, scale=scale)
                        last.then_inc(qk32_ready, 1)

            run_phases(act, phase)

        @block.vector
        def _(dve):
            def carry():
                at = next(carried_v) % CARRIERS
                dve.memset(carrier_v[:, at:at + 1], 0.0)

            dve.wait_ge(consts_in, 96)
            dve.tensor_scalar(bq_cols[:, :], bq_raw[:, :], SCALE[0], None, ALU.mult).then_inc(bq_ready, 1)
            for m in range(3):
                dve.wait_ge(w_hi_ready, m + 1)
                dve.scalar_tensor_tensor(w_lo[m][:, :, :], staging(m), W_SCALE, w_hi[m][:, :, :],
                                         ALU.mult, ALU.subtract).then_inc(w_lo_ready, 1)
            for m in range(3, 7):
                for c in range(KC):
                    n = (m - 3) * KC + c
                    dve.wait_ge(w_hi_ready, 3 + n + 1)
                    dve.scalar_tensor_tensor(w_lo[m][:, c, :], WT_BANKS[n % 4][:, 0:DIM], W_SCALE,
                                             w_hi[m][:, c, :], ALU.mult, ALU.subtract).then_inc(w_lo_ready, 1)

            def biased_scores(u, c):
                n = chunk(u, c)
                b, first = c // KC, c % KC * HC
                if c % KC == 0 and u.layer == 0:
                    dve.wait_ge(bias_ready, u.group + 1)
                if c == 0 and u.layer == 1:
                    dve.wait_ge(adj1_in, u.group * 16 + 16)
                dve.wait_ge(scores_done, n)
                if some(n - 2):
                    dve.wait_ge(exp_done, n - 2)
                carry()
                bias = (bias0 if u.layer == 0 else adj1)[:, b, :]
                for h in range(HC):
                    last = dve.tensor_tensor_reduce(
                        out=neg[c % 2][:, h, :], in0=score_bank[c % 2][:, P * h:P * (h + 1)], in1=bias,
                        scale=-1.0, scalar=HUGE, op0=ALU.add, op1=ALU.min,
                        accum_out=neg_max[:, b % 2, first + h:first + h + 1])
                last.then_inc(neg_ready, 1)
                if u.layer == 1:
                    dve.wait_ge(neg_ready, n)
                    dve.tensor_reduce(neg_min[:, b % 2, first:first + HC], neg[c % 2][:, :, :], AX.X,
                                      ALU.max).then_inc(min_done, 1)

            def build_bias(g):
                dve.wait_ge(adj0_in, g * 16 + 16)
                dve.tensor_scalar(mask0[:, :, :], adj0[:, :, :], 0.0, MASKED, ALU.is_le,
                                  ALU.mult).then_inc(bias_parts, 1)
                dve.tensor_scalar(scaled0[:, :, :], adj0[:, :, :], 0.0, beta_all[:, 0:1], ALU.max,
                                  ALU.mult).then_inc(bias_parts, 1)
                dve.wait_ge(bias_parts, g * 2 + 2)
                dve.tensor_tensor(bias0[:, :, :], mask0[:, :, :], scaled0[:, :, :], ALU.add).then_inc(bias_ready, 1)

            def norm_stats(u, b):
                n = u.n * GROUP + b
                source = x_norm if u.layer == 0 else x_mid
                if u.layer == 0:
                    dve.wait_ge(x_norm_in, u.group * 16 + 16)
                else:
                    dve.wait_ge(x_mid_ready, u.group * GROUP + (b + 1))
                dve.bn_stats(stats[:, :], source[:, b, :]).then_inc(stats_done, 1)
                dve.wait_ge(stats_done, n + 1)
                carry()
                dve.bn_aggr(moments[:, :], stats[:, :]).then_inc(moments_done, 1)
                if some(n - 1):
                    dve.wait_ge(normed_ready, n - 1)
                dve.wait_ge(moments_done, n + 1)
                dve.tensor_scalar(shift_var[:, b % 2, 0:1], moments[:, 0:1], -1.0, None, ALU.mult)
                dve.tensor_scalar(shift_var[:, b % 2, 1:2], moments[:, 1:2], EPS, None,
                                  ALU.add).then_inc(shift_ready, 1)

            def inverse_sums(u, b):
                dve.wait_ge(exp_done, chunk(u, b * KC + KC - 1))
                n = u.group * GROUP + (b + 1)
                if u.layer == 0:
                    dve.reciprocal(inv0[:, b % 2, :], total[:, b % 2, :]).then_inc(inv0_ready, 1)
                    return
                dve.reciprocal(inv1[:, :], total[:, b % 2, :]).then_inc(inv1_done, 1)
                dve.wait_ge(min_done, u.group * SLOTS + (b * KC + KC))
                dve.tensor_scalar(alive[:, :], neg_max[:, b % 2, :], 0.0, None, ALU.not_equal).then_inc(alive_done, 1)
                dve.wait_ge(alive_done, n)
                dve.scalar_tensor_tensor(live[:, :], neg_min[:, b % 2, :], 0.0, alive[:, :], ALU.not_equal,
                                         ALU.max).then_inc(live_done, 1)
                dve.wait_ge(live_done, n)
                dve.wait_ge(inv1_done, n)
                if some(n - 1):
                    dve.wait_ge(inv_turned, n - 1)
                dve.tensor_tensor(inv_live[:, :], inv1[:, :], live[:, :], ALU.mult).then_inc(inv_live_done, 1)
                dve.wait_ge(inv_live_done, n)
                dve.tensor_copy(inv_wide[:, :, :],
                                inv_live[:, :].unsqueeze(2).to_broadcast([P, HEADS, HEAD])).then_inc(inv_wide_ready, 1)

            def take_v(u, b):
                dve.wait_ge(job_done, u.n * JOBS + (2 * KC + b + 1))
                if some(u.n * SLOTS - SLOTS):
                    dve.wait_ge(pv_done, u.n * SLOTS - SLOTS)
                dve.scalar_tensor_tensor(v32[u.parity][:, b, :], job_bank[b % 2][:, 0:DIM], 1.0 / W_SCALE,
                                         bv_rows[u.layer][:, :], ALU.mult, ALU.add).then_inc(v_ready, 1)

            def phase(p):
                bias_slot = SLOTS - 1 if p.attend is not None and p.attend.layer == 0 else 7
                for s in range(SLOTS):
                    if p.bias is not None and s == bias_slot:
                        build_bias(p.bias)
                    if p.project is not None and s in (8, 9, 11):
                        take_v(p.project, {8: 0, 9: 1, 11: 2}[s])
                    u, c = unit_of_chunk(p, s + 1)
                    if u is not None:
                        biased_scores(u, c)
                    u, b = finished(p, s, 1)
                    if u is not None:
                        inverse_sums(u, b)
                    if s % KC == 0 and p.norm is not None:
                        norm_stats(p.norm, s // KC)
                    u, b = finished(p, s, 3)
                    if u is not None and u.layer == 1:
                        if some(u.n * GROUP + b):
                            dve.wait_ge(post_done, u.n * GROUP + b)
                        dve.wait_ge(o_norm_ready, u.group * GROUP + (b + 1))
                        dve.tensor_copy(o_hi[:, :, :], o_norm[:, :, :]).then_inc(o_hi_ready, 1)
                    u, b = finished(p, s, 2)
                    if u is not None and u.layer == 0:
                        dve.wait_ge(post_done, u.n * GROUP + (b + 1))
                        dve.wait_ge(inv0_ready, u.group * GROUP + (b + 1))
                        if some(u.group * GROUP + b):
                            dve.wait_ge(x_mid_ready, u.group * GROUP + b)
                        dve.tensor_tensor(o_rows[:, :, :], misc_bank[:, 0:DIM].rearrange("p (h d) -> p h d", h=HEADS),
                                          inv0[:, b % 2, :].unsqueeze(2).to_broadcast([P, HEADS, HEAD]),
                                          ALU.mult).then_inc(post_taken, 1)
                    if u is not None and u.layer == 1:
                        dve.wait_ge(o_taken, u.n * GROUP + (b + 1))
                        dve.wait_ge(inv_turned, u.group * GROUP + (b + 1))
                        if some(u.group * GROUP + b):
                            dve.wait_ge(o_lo_ready, u.group * GROUP + b)
                        dve.tensor_tensor(o_norm[:, :, :].rearrange("p c q -> p (c q)"), misc_bank[:, 0:DIM],
                                          o_t[:, :, :].rearrange("p c q -> p (c q)"), ALU.mult).then_inc(o_norm_ready, 1)
                    u, b = finished(p, s, 4)
                    if u is not None and u.layer == 1:
                        dve.wait_ge(post_done, u.n * GROUP + (b + 1))
                        dve.wait_ge(x_mid_bo_ready, u.group * GROUP + (b + 1))
                        if some(u.group * 16):
                            dve.wait_ge(stored[b], u.group * 16)
                        dve.scalar_tensor_tensor(result[b][:, :], misc_bank[:, 0:DIM], 1.0 / W_SCALE,
                                                 x_mid_bo[:, b, :], ALU.mult, ALU.add).then_inc(post_taken, 1)
                    if s % KC == 2 and p.norm is not None:
                        u, b = p.norm, s // KC
                        dve.wait_ge(h_hi_ready, u.n * GROUP + (b + 1))
                        dve.scalar_tensor_tensor(h_lo[u.parity][:, :, P * b:P * (b + 1)],
                                                 misc_bank[:, 0:DIM].rearrange("p (c n) -> p c n", c=KC), 0.0,
                                                 h_hi[u.parity][:, :, P * b:P * (b + 1)],
                                                 ALU.max, ALU.subtract).then_inc(h_lo_ready, 1)
                    if p.project is not None and 1 <= s < 1 + 2 * KC:
                        u, j = p.project, s - 1
                        dve.wait_ge(qk32_ready, u.n * 2 * KC + (j + 1))
                        if j % KC == 0 and some((u.half + u.parity) * STACK_DMAS * 16):
                            dve.wait_ge(stack_in[j // KC][1 - u.parity], (u.half + u.parity) * STACK_DMAS * 16)
                        dve.tensor_copy(part_hi[j // KC][:, j % KC, :], qk32[j % 2][:, :]).then_inc(part_hi_ready, 1)
                    if p.project is not None and s == 11:
                        take_v(p.project, 3)

            run_phases(dve, phase)

        @block.tensor
        def _(pe):
            pe.wait_ge(ident_ready, 1)
            for m in range(3, 7):
                pe.wait_ge(weight_in[m], 16)
                for c in range(KC):
                    n = (m - 3) * KC + c
                    if n >= 4:
                        pe.wait_ge(w_lo_ready, 3 + n - 3)
                    for r in range(KC):
                        last = pe.transpose(WT_BANKS[n % 4][:, P * r:P * (r + 1)], staging(m)[:, r, P * c:P * (c + 1)],
                                            ident[:, :])
                    last.then_inc(weight_turned, 1)
            pe.wait_ge(w_hi_ready, 3 + 4 * KC)
            pe.wait_ge(w_lo_ready, 3 + 4 * KC)

            def project(u, part):
                j, c = part // KC, part % KC
                if part == 0:
                    pe.wait_ge(h_hi_ready, u.n * GROUP + GROUP)
                    pe.wait_ge(h_lo_ready, u.n * GROUP + GROUP)
                if c == 0:
                    if j < 2:
                        if some(u.n * GROUP - GROUP + (3 + j)):
                            pe.wait_ge(v_ready, u.n * GROUP - GROUP + (3 + j))
                    elif j < 2 * KC + 2:
                        pe.wait_ge(qk32_ready, u.n * 2 * KC + (j - 1))
                    else:
                        pe.wait_ge(v_ready, u.n * GROUP + (j - 2 * KC - 1))
                hi, lo = h_hi[u.parity], h_lo[u.parity]
                if j < 2 * KC:
                    m = u.layer * 3 + j // KC
                    cols = slice(P * (j % KC), P * (j % KC + 1))
                    pairs = ((w_hi[m][:, c, cols], hi[:, c, :]), (w_hi[m][:, c, cols], lo[:, c, :]),
                             (w_lo[m][:, c, cols], hi[:, c, :]))
                    to = job_bank[j % 2][:, :]
                else:
                    m = u.layer * 3 + 2
                    b = j - 2 * KC
                    rows = slice(P * b, P * (b + 1))
                    pairs = ((hi[:, c, rows], w_hi[m][:, c, :]), (hi[:, c, rows], w_lo[m][:, c, :]),
                             (lo[:, c, rows], w_hi[m][:, c, :]))
                    to = job_bank[j % 2][:, 0:DIM]
                for n, (stationary, moving) in enumerate(pairs):
                    last = pe.matmul(to, stationary, moving, start=(c == 0 and n == 0), stop=(c == KC - 1 and n == 2))
                if c == KC - 1:
                    last.then_inc(job_done, 1)

            def scores(u, c):
                n = chunk(u, c)
                if c == 0:
                    pe.wait_ge(stack_in[0][u.parity], u.half * STACK_DMAS * 16 + STACK_DMAS * 16)
                    pe.wait_ge(stack_in[1][u.parity], u.half * STACK_DMAS * 16 + STACK_DMAS * 16)
                if some(n - 2):
                    pe.wait_ge(neg_ready, n - 2)
                nodes = slice(P * (c // KC), P * (c // KC + 1))
                q, k = stacked[0][u.parity], stacked[1][u.parity]
                for h in range(HC):
                    last = pe.matmul(score_bank[c % 2][:, P * h:P * (h + 1)], q[0:3 * HEAD, h, c % KC, nodes],
                                     k[0:3 * HEAD, h, c % KC, nodes], start=True, stop=True)
                last.then_inc(scores_done, 1)

            def turn_probs(u, c):
                n = chunk(u, c)
                pe.wait_ge(exp_done, n)
                if some(n - 2):
                    pe.wait_ge(probs_t_ready, n - 2)
                for h in range(HC):
                    last = pe.transpose(pt_bank[c % 2][:, P * h:P * (h + 1)], probs[c % 2][:, h, :], ident[:, :])
                last.then_inc(probs_turned, 1)

            def weigh_values(u, c):
                n = chunk(u, c)
                b = c // KC
                pe.wait_ge(probs_t_ready, n)
                if c % KC == 0:
                    pe.wait_ge(v_ready, u.n * GROUP + (b + 1))
                    if some(u.n * GROUP + b):
                        pe.wait_ge(o_taken, u.n * GROUP + b)
                for h in range(HC):
                    f = P * (c % KC) + HEAD * h
                    last = pe.matmul(o_bank[HEAD * h:HEAD * (h + 1), P * (c % KC):P * (c % KC + 1)],
                                     v32[u.parity][:, b, f:f + HEAD], probs_t[c % 2][:, h, :], start=True, stop=True)
                last.then_inc(pv_done, 1)

            def phase(p):
                for s in range(SLOTS):
                    u, c = unit_of_chunk(p, s + 1)
                    if u is not None:
                        scores(u, c)
                    parts = range(3 * s, 3 * s + 3) if s < 2 * KC else range(2 * s + 6, 2 * s + 8)
                    if p.project is not None:
                        for part in parts[:1]:
                            project(p.project, part)
                    u, c = unit_of_chunk(p, s - 1)
                    if u is not None:
                        weigh_values(u, c)
                    u, b = finished(p, s, 4)
                    if u is not None and u.layer == 1:
                        if p.norm is not None and some(p.norm.n * GROUP + s // KC):
                            pe.wait_ge(h_lo_ready, p.norm.n * GROUP + s // KC)
                        pe.wait_ge(o_hi_ready, u.group * GROUP + (b + 1))
                        pe.wait_ge(o_lo_ready, u.group * GROUP + (b + 1))
                        for c in range(KC):
                            for n, (left, right) in enumerate(((o_hi, w_hi), (o_hi, w_lo), (o_lo, w_hi))):
                                last = pe.matmul(misc_bank[:, 0:DIM], left[:, c, :], right[6][:, c, :],
                                                 start=(c == 0 and n == 0), stop=(c == KC - 1 and n == 2))
                        last.then_inc(post_done, 1)
                    u, b = finished(p, s, 2)
                    if u is not None:
                        if p.norm is not None and some(p.norm.n * GROUP + s // KC):
                            pe.wait_ge(h_lo_ready, p.norm.n * GROUP + s // KC)
                        if some(u.n * GROUP + b):
                            pe.wait_ge(post_taken, u.n * GROUP + b)
                    if u is not None and u.layer == 0:
                        pe.wait_ge(o_taken, u.n * GROUP + (b + 1))
                        for c in range(KC):
                            last = pe.transpose(misc_bank[:, P * c:P * (c + 1)], o_t[:, c, :], ident[:, :])
                        last.then_inc(post_done, 1)
                    if u is not None and u.layer == 1:
                        pe.wait_ge(inv_wide_ready, u.group * GROUP + (b + 1))
                        for c in range(KC):
                            last = pe.transpose(misc_bank[:, P * c:P * (c + 1)],
                                                inv_wide[:, HC * c:HC * (c + 1), :].rearrange("p h d -> p (h d)"),
                                                ident[:, :])
                        last.then_inc(inv_turned, 1)
                    if s % KC == 2 and p.norm is not None:
                        before_u, before_b = finished(p, s, 3)
                        if before_u is not None and before_u.layer == 1:
                            pe.wait_ge(o_norm_ready, before_u.group * GROUP + (before_b + 1))
                        if before_u is not None and before_u.layer == 0:
                            pe.wait_ge(post_taken, before_u.n * GROUP + (before_b + 1))
                        u, b = p.norm, s // KC
                        if some(u.n * GROUP + b):
                            pe.wait_ge(h_lo_ready, u.n * GROUP + b)
                        pe.wait_ge(normed_ready, u.n * GROUP + (b + 1))
                        for c in range(KC):
                            last = pe.transpose(misc_bank[:, P * c:P * (c + 1)], normed[b % 2][:, P * c:P * (c + 1)],
                                                ident[:, :])
                        last.then_inc(h_turned, 1)
                    if p.project is not None:
                        for part in parts[1:]:
                            project(p.project, part)
                    if p.attend is not None:
                        turn_probs(p.attend, s)

            run_phases(pe, phase)


NAMES = ("x", "adj", "L0_gnn_Wq", "L0_gnn_bq", "L0_gnn_Wk", "L0_gnn_bk", "L0_gnn_Wv", "L0_gnn_bv", "L0_gnn_beta",
         "L1_gnn_Wq", "L1_gnn_Wk", "L1_gnn_Wv", "L1_gnn_bv", "L1_gnn_Wo", "L1_gnn_bo")


def kernel(**inputs):
    import concourse.bacc as bacc
    import numpy as np
    from concourse.bass_utils import run_bass_kernel_spmd

    nc = bacc.Bacc("TRN2", target_bir_lowering=False, num_devices=1)
    arrays, args = {}, []
    for name in NAMES:
        a = np.ascontiguousarray(inputs[name])
        if name == "L0_gnn_beta":
            a = a.reshape(1, 1)
        arrays[f"in_{name}"] = a
        args.append(nc.dram_tensor(f"in_{name}", a.shape, mybir.dt.from_np(a.dtype), kind="ExternalInput").ap())
    args.append(nc.dram_tensor("out_x", (GRAPHS, NODES, DIM), F32, kind="ExternalOutput").ap())
    build(nc, *args)
    done = run_bass_kernel_spmd(nc, [arrays], core_ids=[0])
    return done.results[0]["out_x"]
```
